# Optimizing a Trainium2 kernel written in Bass

```python
import numpy as np
import jax
import jax.numpy as jnp

def _softmax(x, axis=-1):
    return jax.nn.softmax(x, axis=axis)

def _gelu(x):
    return jax.nn.gelu(x, approximate=True)

def _silu(x):
    return jax.nn.silu(x)

def _sigmoid(x):
    return jax.nn.sigmoid(x)

def _layernorm(x, axis=-1, eps=1e-05):
    m = jnp.mean(x, axis=axis, keepdims=True)
    v = jnp.var(x, axis=axis, keepdims=True)
    return (x - m) / jnp.sqrt(v + eps)

def _scatter_add(tgt, idx, src, axis=0):
    return tgt.at[idx].add(src)

def _segment_sum(src, seg, n):
    return jax.ops.segment_sum(src, seg, n)
kernel_name = 'mk_rec_standalone_d1_rec_r8_f2e3e9'

def setup_inputs(seed: int=0):
    np.random.seed(seed)
    _w = jnp.asarray

    def _rec_inputs():
        import jax
        import jax.numpy as jnp
        _rk = jax.random.key(seed)
        r_sequence_ids = jax.random.randint(jax.random.fold_in(_rk, 1), (512, 200), 35, 109962, jnp.int32)
        return r_sequence_ids
    r_sequence_ids = _rec_inputs()

    def _L0_rec_setup():
        import jax, jax.numpy as jnp
        import numpy as np
        N_ITEMS = 12500
        HIDDEN = 512
        BATCH = 64
        SEQ = 200
        key = jax.random.key(seed)
        k1, k2, k3 = jax.random.split(key, 3)
        sequence_ids = jax.random.randint(k1, (BATCH, SEQ), 0, 13750, dtype=jnp.int64 if jax.config.jax_enable_x64 else jnp.int32)
        emb_table = jax.random.normal(k2, (N_ITEMS, HIDDEN), dtype=jnp.float32) * 0.02
        proj_w = jax.random.normal(k3, (HIDDEN, N_ITEMS), dtype=jnp.float32) * 0.02
        proj_b = jnp.zeros((N_ITEMS,), dtype=jnp.float32)
        return {'sequence_ids': sequence_ids, 'emb_table': emb_table, 'proj_w': proj_w, 'proj_b': proj_b}
    _L0_rec_all = _L0_rec_setup()
    _L0_rec_in = {k: v for k, v in _L0_rec_all.items() if k in ('emb_table', 'proj_w', 'proj_b')}
    del _L0_rec_all
    return {'r_sequence_ids': r_sequence_ids, 'L0_rec_emb_table': _L0_rec_in['emb_table'], 'L0_rec_proj_w': _L0_rec_in['proj_w'], 'L0_rec_proj_b': _L0_rec_in['proj_b']}

def reference(r_sequence_ids, L0_rec_emb_table, L0_rec_proj_w, L0_rec_proj_b):
    import jax
    import jax.numpy as jnp

    def _L0_rec_ref(sequence_ids, emb_table, proj_w, proj_b):
        import jax, jax.numpy as jnp
        import numpy as np
        N_ITEMS = 12500
        HIDDEN = 512
        BATCH = 64
        SEQ = 200
        valid = sequence_ids < emb_table.shape[0]
        safe_ids = jnp.where(valid, sequence_ids, 0)
        seq_emb = emb_table[safe_ids]
        seq_emb = seq_emb * valid[..., None].astype(seq_emb.dtype)
        denom = jnp.maximum(valid.sum(axis=1, keepdims=True).astype(seq_emb.dtype), 1.0)
        user_repr = seq_emb.sum(axis=1) / denom
        logits = user_repr @ proj_w + proj_b
        return logits
    y = _L0_rec_ref(r_sequence_ids, L0_rec_emb_table, L0_rec_proj_w, L0_rec_proj_b)
    return y

_drawn_inputs = setup_inputs


def setup_inputs(seed=0):
    import zlib

    import numpy as np

    out = dict(_drawn_inputs(seed))
    spreads = {'L0_rec_proj_b': (0.0, 0.1)}
    factors = {'L0_rec_emb_table': 2.919, 'L0_rec_proj_w': 2.915}
    for name, (base, spread) in spreads.items():
        noise = np.random.default_rng([zlib.crc32(name.encode()), seed]).standard_normal(out[name].shape)
        drawn = base * np.exp(spread * noise) if base else spread * noise
        out[name] = jnp.asarray(drawn.astype(out[name].dtype))
    for name, factor in factors.items():
        out[name] = (out[name] * factor).astype(out[name].dtype)
    return out
```

```python
from contextlib import ExitStack

import concourse.bass as bass
from concourse import mybir

ALU = mybir.AluOpType
ACT = mybir.ActivationFunctionType
AX = mybir.AxisListType
F32 = mybir.dt.float32
F32R = mybir.dt.float32r
I32 = mybir.dt.int32
U32 = mybir.dt.uint32

P = 128
TILES_PER_PASS = 2
SLOTS = 8
GROUP = 4
RING = 5
LOW = 32


def build_program(nc, ids_dram, table_dram, weight_dram, bias_dram, out_dram):
    users, seq = ids_dram.shape
    items, hidden = table_dram.shape
    tiles = users // P
    passes = tiles // TILES_PER_PASS
    depth = hidden // P
    chunk = items // (RING * RING)
    steps = items // (chunk * RING)
    rows_out = TILES_PER_PASS * P
    assert chunk * RING * steps == items and chunk <= 512 and chunk % 2 == 0 and passes == 2

    with ExitStack() as ctx:
        def sb(name, shape, dt):
            return ctx.enter_context(nc.sbuf_tensor(name, shape, dt))

        def ps(name, shape):
            return ctx.enter_context(nc.psum_tensor(name, shape, F32))

        def sem(name):
            return ctx.enter_context(nc.semaphore(name))

        ids = sb("ids", [P, tiles, seq], I32)
        keys = sb("keys", [P, tiles, seq], F32)
        top = sb("top", [P, passes, TILES_PER_PASS, SLOTS], F32)
        pick = sb("pick", [P, passes, TILES_PER_PASS, SLOTS], I32)
        keep = sb("keep", [P, passes, TILES_PER_PASS, SLOTS], F32)
        first = sb("first", [P, passes, TILES_PER_PASS, SLOTS], F32)
        count = sb("count", [P, tiles], F32)
        denom = sb("denom", [P, tiles], F32)
        share = sb("share", [P, tiles], F32)
        most = sb("most", [1, passes], F32)
        most_up = sb("most_up", [1, passes], I32)
        rounds = sb("rounds", [1, passes], I32)
        valid = ids[:, :, :].bitcast(F32)

        rows = sb("rows", [P, TILES_PER_PASS, SLOTS, hidden], F32)
        acc = sb("acc", [P, TILES_PER_PASS, 2, hidden], F32)
        user_hi = sb("user_hi", [P, passes, TILES_PER_PASS, depth, P], F32R)
        user_lo = sb("user_lo", [P, passes, TILES_PER_PASS, depth, P], F32R)

        w_raw = sb("w_raw", [P, RING, depth, chunk], F32)
        w_hi = sb("w_hi", [P, RING, depth, chunk], F32R)
        w_lo = sb("w_lo", [P, RING, depth, chunk], F32R)
        out_sb = sb("out_sb", [P, RING, chunk], F32)
        bias_parts = sb("bias_parts", [P, steps, chunk], F32R)
        bias_raw = out_sb[:, :, :].rearrange("p a n -> p (a n)").rearrange("p (a n) -> p a n", n=chunk)
        pick_row = sb("pick_row", [P, RING, P], F32R)
        ramp = acc[:, 0, :, :].rearrange("p a n -> p (a n)")[:, 0:RING * P].bitcast(I32)
        pick_low = acc[:, 1, :, :].rearrange("p a n -> p (a n)")[:, 0:RING * P]
        ramp_sq = acc[:, 1, :, :].rearrange("p a n -> p (a n)")[:, RING * P:RING * P + P].bitcast(I32)
        ident = sb("ident", [P, P], F32)

        out_ps = [ps(f"out_ps{b}", [P, chunk]) for b in range(RING)]
        user_ps = [ps(f"user_ps{t}", [P, depth, P]) for t in range(TILES_PER_PASS)]
        count_ps = ps("count_ps", [P, tiles * P])

        ids_landed = sem("ids_landed")
        bias_landed = sem("bias_landed")
        ramps_made = sem("ramps_made")
        keys_made = sem("keys_made")
        counted = sem("counted")
        count_steps = sem("count_steps")
        bias_cleared = sem("bias_cleared")
        pick_row_steps = sem("pick_row_steps")
        ident_made = sem("ident_made")
        bias_rounded = sem("bias_rounded")
        counts_turned = sem("counts_turned")
        rounds_ready = sem("rounds_ready")
        sorted_steps = [sem(f"sorted_steps{p}") for p in range(passes)]
        picks_ready = [[[sem(f"picks_ready{p}_{t}_{g}") for g in range(2)] for t in range(2)] for p in range(passes)]
        row_landed = [[[sem(f"row_landed{p}_{t}_{k}") for k in range(SLOTS)] for t in range(2)] for p in range(passes)]
        groups_started = sem("groups_started")
        rows_added = [sem(f"rows_added{p}") for p in range(passes)]
        mean_steps = [sem(f"mean_steps{p}") for p in range(passes)]
        mean_turned = [[sem(f"mean_turned{p}_{t}") for t in range(2)] for p in range(passes)]
        user_hi_ready = [[sem(f"user_hi_ready{p}_{t}") for t in range(2)] for p in range(passes)]
        user_lo_ready = [[sem(f"user_lo_ready{p}_{t}") for t in range(2)] for p in range(passes)]
        w_landed = [sem(f"w_landed{j}") for j in range(RING)]
        w_hi_ready = [sem(f"w_hi_ready{j}") for j in range(RING)]
        w_lo_ready = [sem(f"w_lo_ready{j}") for j in range(RING)]
        out_summed = [sem(f"out_summed{b}") for b in range(RING)]
        out_copied = [sem(f"out_copied{b}") for b in range(RING)]
        out_stored = [sem(f"out_stored{b}") for b in range(RING)]

        w_view = weight_dram.rearrange("(k p) n -> p k n", p=P)
        bias_view = bias_dram.rearrange("(i j n) -> j i n", j=RING, n=chunk)
        block = ctx.enter_context(nc.Block())

        def place(j, t):
            n = TILES_PER_PASS * j + t
            return n % RING, n // RING

        @block.sync
        def _(sp):
            sp.dma_start(ids[:, :, :], ids_dram.rearrange("(t p) s -> p t s", p=P)).then_inc(ids_landed, 16)
            sp.dma_start(bias_raw[0:RING], bias_view).then_inc(bias_landed, 16)
            sp.dma_start(bias_raw[LOW:LOW + RING], bias_view).then_inc(bias_landed, 16)
            for j in range(RING):
                sp.dma_start(w_raw[:, j], w_view[:, :, j * chunk:(j + 1) * chunk]).then_inc(w_landed[j], 16)
            for p in range(passes):
                with sp.Fori(0 if p else 1, steps) as i:
                    for j in range(RING):
                        sp.wait_ge(w_hi_ready[j], i + p * steps)
                        sp.wait_ge(w_lo_ready[j], i + p * steps)
                        sp.dma_start(w_raw[:, j], w_view[:, :, bass.ds(i * (RING * chunk) + j * chunk, chunk)]
                                     ).then_inc(w_landed[j], 16)

        @block.gpsimd
        def _(pool):
            pool.iota(ramp.rearrange("p (j m) -> p j m", m=P), [[-1, RING], [0, P]], base=0,
                      channel_multiplier=1).then_inc(ramps_made, 1)
            pool.iota(ramp_sq, [[-1, P]], base=0, channel_multiplier=1).then_inc(ramps_made, 1)

            def gather_group(p, r, t, g):
                pool.wait_ge(picks_ready[p][t][g], r + 1)
                pool.sem_inc(groups_started, 1)
                for k in range(g * GROUP, (g + 1) * GROUP):
                    pool.indirect_dma_start(
                        rows[:, t, k, :], None, table_dram,
                        bass.IndirectOffsetOnAxis(pick[:, p, t, k:k + 1].bitcast(U32), 0),
                        bounds_check=items - 1, oob_is_err=False).then_inc(row_landed[p][t][k], 16)

            def gather_round(p, r):
                for g in range(2):
                    for t in range(TILES_PER_PASS):
                        gather_group(p, r, t, g)

            gather_round(0, 0)
            pool.wait_ge(rounds_ready, 1)
            rounds_of = [pool.value_load(rounds[0:1, p:p + 1], min_val=2, max_val=seq // SLOTS)
                         for p in range(passes)]
            with pool.Fori(1, rounds_of[0]) as r:
                gather_round(0, r)
            pool.wait_ge(mean_steps[0], 1)
            gather_round(1, 0)
            with pool.Fori(1, steps) as r:
                gather_round(1, r)
            with pool.If(rounds_of[1] > steps):
                with pool.Fori(steps, rounds_of[1]) as r:
                    gather_round(1, r)

        @block.tensor
        def _(pe):
            pe.wait_ge(counted, 2)
            pe.wait_ge(ident_made, 1)
            for t in range(tiles):
                mm = pe.matmul(count_ps[0:1, t * P:(t + 1) * P], count[:, t:t + 1], ident[:, :],
                               start=True, stop=True)
            mm.then_inc(counts_turned, 1)

            for p in range(passes):
                for t in range(TILES_PER_PASS):
                    pe.wait_ge(mean_steps[p], 4)
                    for k in range(depth):
                        mm = pe.transpose(user_ps[t][:, k, :], acc[:, t, 0, k * P:(k + 1) * P], ident[:, :])
                    mm.then_inc(mean_turned[p][t], 1)
                if p == 0:
                    pe.wait_ge(bias_rounded, 3)
                    pe.wait_ge(pick_row_steps, 2)
                for t in range(TILES_PER_PASS):
                    pe.wait_ge(user_hi_ready[p][t], 1)
                    pe.wait_ge(user_lo_ready[p][t], 1)
                with pe.Fori(0, steps) as i:
                    for j in range(RING):
                        pe.wait_ge(w_hi_ready[j], i + p * steps + 1)
                        pe.wait_ge(w_lo_ready[j], i + p * steps + 1)
                        for t in range(TILES_PER_PASS):
                            b, before = place(j, t)
                            pe.wait_ge(out_copied[b], 2 * i + 2 * p * steps + before + 1)
                            pe.matmul(out_ps[b][:, :], pick_row[:, j, :],
                                      bias_parts[:, :, :].rearrange("p i n -> p (i n)")[:, bass.ds(i * chunk, chunk)],
                                      start=True, stop=False)
                            for k in range(depth):
                                hi, lo = user_hi[:, p, t, k, :], user_lo[:, p, t, k, :]
                                pe.matmul(out_ps[b][:, :], hi, w_hi[:, j, k, :], start=False, stop=False)
                                pe.matmul(out_ps[b][:, :], hi, w_lo[:, j, k, :], start=False, stop=False)
                                mm = pe.matmul(out_ps[b][:, :], lo, w_hi[:, j, k, :],
                                               start=False, stop=(k == depth - 1))
                            mm.then_inc(out_summed[b], 1)

        @block.scalar
        def _(act):
            for b in range(RING):
                act.sem_inc(out_copied[b], 1)
                act.sem_inc(out_stored[b], 16)
            act.wait_ge(bias_cleared, 1)
            act.wait_ge(bias_landed, 32)
            for lo in (0, LOW):
                act.activation(bias_parts[lo:lo + RING], bias_raw[lo:lo + RING], ACT.Copy).then_inc(bias_rounded, 1)

            def take_high(m, j):
                act.wait_ge(w_landed[j], 16 * m + 16)
                if not (isinstance(m, int) and m == 0):
                    b, before = place(j, TILES_PER_PASS - 1)
                    act.wait_ge(out_summed[b], 2 * m - 1 + before)
                act.activation(w_hi[:, j], w_raw[:, j], ACT.Copy).then_inc(w_hi_ready[j], 1)

            def put_out(p, i, j):
                m = i + p * steps
                for t in range(TILES_PER_PASS):
                    b, before = place(j, t)
                    act.wait_ge(out_summed[b], 2 * m + before + 1)
                    act.wait_ge(out_stored[b], 32 * m + 16 * before + 16)
                    act.activation(out_sb[:, b, :], out_ps[b][:, :], ACT.Copy).then_inc(out_copied[b], 1)
                for t in range(TILES_PER_PASS):
                    b, before = place(j, t)
                    act.wait_ge(out_copied[b], 2 * m + before + 2)
                    act.dma_start(out_dram[p * rows_out + t * P:p * rows_out + (t + 1) * P,
                                           bass.ds(i * (RING * chunk) + j * chunk, chunk)],
                                  out_sb[:, b, :]).then_inc(out_stored[b], 16)

            for j in range(RING):
                take_high(0, j)
            act.wait_ge(bias_rounded, 3)
            for p in range(passes):
                for t in range(TILES_PER_PASS):
                    act.wait_ge(mean_turned[p][t], 1)
                    act.activation(user_hi[:, p, t], user_ps[t][:, :, :], ACT.Copy).then_inc(user_hi_ready[p][t], 1)
                with act.Fori(0, steps - 1) as i:
                    for j in range(RING):
                        take_high(i + p * steps + 1, j)
                        put_out(p, i, j)
                for j in range(RING):
                    if p < passes - 1:
                        take_high((p + 1) * steps, j)
                    put_out(p, steps - 1, j)
            for b in range(RING):
                act.wait_ge(out_stored[b], 32 * passes * steps + 16)

        @block.vector
        def _(dve):
            taken = [[0], [0]]

            def step(p, ins):
                taken[p][0] += 1
                ins.then_inc(sorted_steps[p], 1)

            def settled(p, base=0):
                dve.wait_ge(sorted_steps[p], base + taken[p][0])

            def refill(p, t, g, base=0, source=None):
                s = slice(g * GROUP, (g + 1) * GROUP)
                tile = keys[:, p * TILES_PER_PASS + t, :]
                dve.tensor_scalar(pick[:, p, t, s], top[:, p, t, s] if source is None else source, -1.0, float(items),
                                  ALU.mult, ALU.add).then_inc(picks_ready[p][t][g], 1)
                if g == 1:
                    step(p, dve.match_replace(tile, top[:, p, t, :], tile, 0.0))
                if g == 1 and source is None:
                    settled(p, base)
                    step(p, dve.tensor_scalar(keep[:, p, t, s], pick[:, p, t, s], float(items), None, ALU.is_lt))
                else:
                    step(p, dve.tensor_scalar(keep[:, p, t, s], top[:, p, t, s], 0.0, None, ALU.is_gt))
                if g == 1 and source is not None:
                    settled(p, base)
                if g == 1:
                    step(p, dve.max(top[:, p, t, :], tile))

            ROUND_STEPS = 8

            def first_picks(p):
                for t in range(TILES_PER_PASS):
                    step(p, dve.max(top[:, p, t, :], keys[:, p * TILES_PER_PASS + t, :]))
                for t in range(TILES_PER_PASS):
                    settled(p)
                    step(p, dve.tensor_scalar(first[:, p, t, :], top[:, p, t, :], 1.0, None, ALU.max))
                    settled(p)
                    for g in range(2):
                        refill(p, t, g, source=first[:, p, t, g * GROUP:(g + 1) * GROUP])

            def add_group(p, r, t, g):
                added = 2 * SLOTS * r + g * TILES_PER_PASS * GROUP + t * GROUP
                settled(p, r * ROUND_STEPS)
                for k in range(g * GROUP, (g + 1) * GROUP):
                    row, weight, total = rows[:, t, k, :], keep[:, p, t, k:k + 1], acc[:, t, k % 2, :]
                    dve.wait_ge(row_landed[p][t][k], 16 * r + 16)
                    if isinstance(r, int) and r == 0 and k < 2:
                        dve.tensor_scalar(total, row, weight, None, ALU.mult).then_inc(rows_added[p], 1)
                    else:
                        dve.wait_ge(rows_added[p], added - 1)
                        dve.scalar_tensor_tensor(out=total, in0=row, scalar=weight, in1=total,
                                                 op0=ALU.mult, op1=ALU.add).then_inc(rows_added[p], 1)
                    added = added + 1
                dve.wait_ge(rows_added[p], added)
                refill(p, t, g, r * ROUND_STEPS)

            def add_round(p, r):
                for g in range(2):
                    for t in range(TILES_PER_PASS):
                        add_group(p, r, t, g)

            def loop_round(p, r):
                at = taken[p][0]
                add_round(p, r)
                taken[p][0] = at

            def take_low(m, j):
                dve.wait_ge(w_hi_ready[j], m + 1)
                dve.tensor_tensor(w_lo[:, j], w_raw[:, j], w_hi[:, j].bitcast(F32), ALU.subtract
                                  ).then_inc(w_lo_ready[j], 1)

            def mean_of(p):
                for t in range(TILES_PER_PASS):
                    dve.tensor_tensor(acc[:, t, 0, :], acc[:, t, 0, :], acc[:, t, 1, :], ALU.add
                                      ).then_inc(mean_steps[p], 1)
                for t in range(TILES_PER_PASS):
                    dve.wait_ge(mean_steps[p], t + 1)
                    dve.tensor_scalar(acc[:, t, 0, :], acc[:, t, 0, :],
                                      share[:, p * TILES_PER_PASS + t:p * TILES_PER_PASS + t + 1], None, ALU.mult
                                      ).then_inc(mean_steps[p], 1)
                for t in range(TILES_PER_PASS):
                    dve.wait_ge(user_hi_ready[p][t], 1)
                    dve.tensor_tensor(user_lo[:, p, t], user_ps[t][:, :, :], user_hi[:, p, t].bitcast(F32), ALU.subtract
                                      ).then_inc(user_lo_ready[p][t], 1)

            dve.wait_ge(ids_landed, 16)
            dve.tensor_scalar(keys[:, :, :], ids[:, :, :], -1.0, float(items), ALU.mult, ALU.add).then_inc(keys_made, 1)
            dve.wait_ge(keys_made, 1)
            dve.tensor_scalar(valid, keys[:, :, :], 0.0, None, ALU.is_gt).then_inc(counted, 1)
            first_picks(0)
            dve.wait_ge(counted, 1)
            dve.tensor_reduce(count[:, :], valid, AX.X, ALU.add).then_inc(counted, 1)
            dve.wait_ge(ramps_made, 2)
            dve.tensor_scalar(ident[:, :], ramp_sq, 0.0, None, ALU.is_equal).then_inc(ident_made, 1)
            first_picks(1)

            dve.tensor_scalar(denom[:, :], count[:, :], 1.0, None, ALU.max).then_inc(count_steps, 1)
            dve.wait_ge(count_steps, 1)
            dve.reciprocal(share[:, :], denom[:, :]).then_inc(count_steps, 1)
            dve.wait_ge(counts_turned, 1)
            dve.tensor_reduce(most[:, :], count_ps[0:1, :].rearrange("o (p u) -> o p u", p=passes), AX.X, ALU.max
                              ).then_inc(count_steps, 1)
            dve.wait_ge(count_steps, 3)
            for p, least in enumerate((2, steps)):
                dve.tensor_scalar(most_up[:, p:p + 1], most[:, p:p + 1], float(least * SLOTS), float(SLOTS - 1),
                                  ALU.max, ALU.add).then_inc(count_steps, 1)
            dve.wait_ge(count_steps, 5)
            dve.tensor_scalar(rounds[:, :], most_up[:, :], SLOTS.bit_length() - 1, None, ALU.logical_shift_right
                              ).then_inc(rounds_ready, 1)

            dve.memset(bias_parts[:, :, :].bitcast(F32), 0.0).then_inc(bias_cleared, 1)
            dve.tensor_scalar(pick_low, ramp, float(LOW), None, ALU.is_equal).then_inc(pick_row_steps, 1)
            dve.wait_ge(pick_row_steps, 1)
            dve.scalar_tensor_tensor(out=pick_row[:, :, :].rearrange("p j m -> p (j m)"), in0=ramp, scalar=0.0,
                                     in1=pick_low, op0=ALU.is_equal, op1=ALU.add).then_inc(pick_row_steps, 1)
            dve.wait_ge(pick_row_steps, 2)
            add_round(0, 0)
            dve.wait_ge(bias_rounded, 2)
            low = slice(LOW, LOW + RING)
            dve.tensor_tensor(bias_parts[low], bias_raw[low], bias_parts[low].bitcast(F32), ALU.subtract
                              ).then_inc(bias_rounded, 1)
            for j in range(2):
                take_low(0, j)

            dve.wait_ge(rounds_ready, 1)
            rounds_of = [dve.value_load(rounds[0:1, p:p + 1], min_val=2, max_val=seq // SLOTS)
                         for p in range(passes)]
            taken[0][0] -= ROUND_STEPS
            with dve.Fori(1, rounds_of[0]) as r:
                loop_round(0, r)
            mean_of(0)
            for j in range(2, RING):
                take_low(0, j)

            def step_of_pass(p, i, last=False):
                at = taken[1][0]
                for j in range(RING):
                    if not last:
                        take_low(i + p * steps + 1, j)
                    if p == 0 and j > 0:
                        add_group(1, i, (j - 1) % 2, (j - 1) // 2)
                taken[1][0] = at

            dve.wait_ge(mean_turned[0][1], 1)
            for j in range(RING):
                take_low(1, j)
                if j > 0:
                    add_group(1, 0, (j - 1) % 2, (j - 1) // 2)
            taken[1][0] -= ROUND_STEPS
            with dve.Fori(1, steps) as i:
                step_of_pass(0, i)
            with dve.If(rounds_of[1] > steps):
                with dve.Fori(steps, rounds_of[1]) as r:
                    loop_round(1, r)
            mean_of(1)
            with dve.Fori(0, steps - 1) as i:
                step_of_pass(1, i)


def kernel(r_sequence_ids, L0_rec_emb_table, L0_rec_proj_w, L0_rec_proj_b):
    import numpy as np
    import concourse.bacc as bacc
    from concourse.bass_utils import run_bass_kernel_spmd

    given = {"ids": r_sequence_ids, "table": L0_rec_emb_table, "weight": L0_rec_proj_w, "bias": L0_rec_proj_b}
    arrays = {f"{name}_dram": np.ascontiguousarray(a) for name, a in given.items()}
    nc = bacc.Bacc("TRN2", target_bir_lowering=False, num_devices=1)
    args = [nc.dram_tensor(name, a.shape, mybir.dt.from_np(a.dtype), kind="ExternalInput").ap()
            for name, a in arrays.items()]
    shape = (arrays["ids_dram"].shape[0], arrays["weight_dram"].shape[1])
    out = nc.dram_tensor("logits_dram", shape, F32, kind="ExternalOutput").ap()
    build_program(nc, *args, out)
    result = run_bass_kernel_spmd(nc, [arrays], core_ids=[0])
    return result.results[0]["logits_dram"]
```

```python
from contextlib import ExitStack

import concourse.bass as bass
from concourse import mybir

ALU = mybir.AluOpType
ACT = mybir.ActivationFunctionType
AX = mybir.AxisListType
F32 = mybir.dt.float32
F32R = mybir.dt.float32r
I32 = mybir.dt.int32
U32 = mybir.dt.uint32

P = 128
PAIR = 2
SLOTS = 8
RING = 5
LOW = 32


def build_program(nc, ids_dram, table_dram, weight_dram, bias_dram, out_dram):
    users, seq = ids_dram.shape
    items, hidden = table_dram.shape
    tiles = users // P
    passes = tiles // PAIR
    depth = hidden // P
    chunk = items // (RING * RING)
    steps = items // (chunk * RING)
    assert chunk * RING * steps == items and chunk <= 512 and chunk % 2 == 0 and passes == 2
    first_rounds = 2
    pair_rounds = steps
    assert max(first_rounds + 1, pair_rounds) * SLOTS <= seq

    with ExitStack() as ctx:
        def sb(name, shape, dt):
            return ctx.enter_context(nc.sbuf_tensor(name, shape, dt))

        def ps(name, shape):
            return ctx.enter_context(nc.psum_tensor(name, shape, F32))

        def sem(name):
            return ctx.enter_context(nc.semaphore(name))

        ids = sb("ids", [P, tiles, seq], I32)
        keys = sb("keys", [P, tiles, seq], F32)
        top = sb("top", [P, tiles, SLOTS], F32)
        pick = sb("pick", [P, tiles, 2, SLOTS], I32)
        keep = sb("keep", [P, tiles, 2, SLOTS], F32)
        first = sb("first", [P, 2, SLOTS], F32)
        count = sb("count", [P, tiles], F32)
        denom = sb("denom", [P, tiles], F32)
        share = sb("share", [P, tiles], F32)
        most = sb("most", [1, 3], F32)
        most_up = sb("most_up", [1, 3], I32)
        rounds = sb("rounds", [1, 3], I32)
        doubles_up = sb("doubles_up", [1, 2], I32)
        doubles = sb("doubles", [1, 2], I32)
        valid = ids[:, :, :].bitcast(F32)

        rows = sb("rows", [P, 2, SLOTS, hidden], F32)
        acc = sb("acc", [P, PAIR, 2, hidden], F32)
        user_hi = sb("user_hi", [P, tiles, depth, P], F32R)
        user_lo = sb("user_lo", [P, tiles, depth, P], F32R)

        w_raw = sb("w_raw", [P, RING, depth, chunk], F32)
        w_hi = sb("w_hi", [P, RING, depth, chunk], F32R)
        w_lo = sb("w_lo", [P, RING, depth, chunk], F32R)
        out_sb = sb("out_sb", [P, RING, chunk], F32)
        bias_parts = sb("bias_parts", [P, steps, chunk], F32R)
        bias_flat = bias_parts[:, :, :].rearrange("p i n -> p (i n)")
        bias_raw = out_sb[:, :, :]
        pick_row = sb("pick_row", [P, RING, P], F32R)
        ident = sb("ident", [P, P], F32)
        ramp = acc[:, 0, :, :].rearrange("p a n -> p (a n)")[:, 0:RING * P].bitcast(I32)
        pick_low = acc[:, 1, :, :].rearrange("p a n -> p (a n)")[:, 0:RING * P]
        ramp_sq = acc[:, 1, :, :].rearrange("p a n -> p (a n)")[:, RING * P:RING * P + P].bitcast(I32)
        bias_wide = rows[:, 0, :, :].rearrange("p k n -> p (k n)")[:, 0:RING * chunk].rearrange(
            "p (j n) -> p j n", n=chunk)

        out_ps = [ps(f"out_ps{b}", [P, chunk]) for b in range(RING)]
        user_ps = [ps(f"user_ps{t}", [P, depth, P]) for t in range(PAIR)]
        count_ps = ps("count_ps", [P, tiles * P])

        ids_landed = sem("ids_landed")
        bias_landed = sem("bias_landed")
        ramps_made = sem("ramps_made")
        keys_made = sem("keys_made")
        counted = sem("counted")
        count_steps = sem("count_steps")
        bias_cleared = sem("bias_cleared")
        pick_row_steps = sem("pick_row_steps")
        ident_made = sem("ident_made")
        bias_rounded = sem("bias_rounded")
        counts_turned = sem("counts_turned")
        rounds_ready = sem("rounds_ready")
        sorted_steps = [sem(f"sorted_steps{q}") for q in range(tiles)]
        picks_ready = [[sem(f"picks_ready{q}_{h}") for h in range(2)] for q in range(tiles)]
        row_landed = [[[sem(f"row_landed{q}_{h}_{k}") for k in range(SLOTS)] for h in range(2)]
                      for q in range(tiles)]
        gathers_started = sem("gathers_started")
        rows_added = [sem(f"rows_added{q}") for q in range(tiles)]
        mean_steps = [sem(f"mean_steps{q}") for q in range(tiles)]
        mean_turned = [sem(f"mean_turned{q}") for q in range(tiles)]
        user_hi_ready = [sem(f"user_hi_ready{q}") for q in range(tiles)]
        user_lo_ready = [sem(f"user_lo_ready{q}") for q in range(tiles)]
        w_landed = [sem(f"w_landed{j}") for j in range(RING)]
        w_hi_ready = [sem(f"w_hi_ready{j}") for j in range(RING)]
        w_lo_ready = [sem(f"w_lo_ready{j}") for j in range(RING)]
        out_summed = [sem(f"out_summed{b}") for b in range(RING)]
        out_copied = [sem(f"out_copied{b}") for b in range(RING)]
        out_stored = [sem(f"out_stored{b}") for b in range(RING)]
        bias_wide_landed = [sem(f"bias_wide_landed{j}") for j in range(RING)]

        w_view = weight_dram.rearrange("(k p) n -> p k n", p=P)
        bias_view = bias_dram.rearrange("(i j n) -> j i n", j=RING, n=chunk)
        bias_line = bias_dram.rearrange("(o n) -> o n", o=1)
        block = ctx.enter_context(nc.Block())

        def place(j, t):
            n = PAIR * j + t
            return n % RING, n // RING

        def place_first(j, t):
            return j, t

        def columns(i, j):
            return bass.ds(i * (RING * chunk) + j * chunk, chunk)

        def columns_back(i, j):
            return bass.ds(i * (-RING * chunk) + ((steps - 1) * RING + j) * chunk, chunk)

        @block.sync
        def _(sp):
            sp.dma_start(ids[:, :, :], ids_dram.rearrange("(t p) s -> p t s", p=P)).then_inc(ids_landed, 16)
            for j in range(RING):
                sp.dma_start(w_raw[:, j], w_view[:, :, columns(0, j)]).then_inc(w_landed[j], 16)
                if j == 0:
                    sp.dma_start(bias_raw[0:RING], bias_view).then_inc(bias_landed, 16)
                    sp.dma_start(bias_raw[LOW:LOW + RING], bias_view).then_inc(bias_landed, 16)

            def load(n, j, at):
                sp.wait_ge(w_hi_ready[j], n)
                sp.wait_ge(w_lo_ready[j], n)
                sp.dma_start(w_raw[:, j], w_view[:, :, at]).then_inc(w_landed[j], 16)

            with sp.Fori(1, steps) as i:
                for j in range(RING):
                    load(i, j, columns(i, j))
            with sp.Fori(1, steps) as i:
                for j in range(RING):
                    load(i + (steps - 1), j, columns_back(i, j))

        @block.gpsimd
        def _(pool):
            pool.memset(bias_parts[:, :, :].bitcast(F32), 0.0).then_inc(bias_cleared, 1)
            pool.iota(ramp_sq, [[-1, P]], base=0, channel_multiplier=1).then_inc(ramps_made, 1)
            pool.iota(ramp.rearrange("p (j m) -> p j m", m=P), [[-1, RING], [0, P]], base=0,
                      channel_multiplier=1).then_inc(ramps_made, 1)

            def gather_round(q, h, used):
                pool.wait_ge(picks_ready[q][h], used + 1)
                pool.sem_inc(gathers_started, 1)
                for k in range(SLOTS):
                    pool.indirect_dma_start(
                        rows[:, h, k, :], None, table_dram,
                        bass.IndirectOffsetOnAxis(pick[:, q, h, k:k + 1].bitcast(U32), 0),
                        bounds_check=items - 1, oob_is_err=False).then_inc(row_landed[q][h][k], 16)

            for q in range(PAIR):
                for h in range(first_rounds):
                    gather_round(q, h, 0)
                if q == 0:
                    pool.wait_ge(rounds_ready, 2)
                    n_rounds = [pool.value_load(rounds[0:1, n:n + 1], min_val=least, max_val=seq // SLOTS)
                                for n, least in enumerate((first_rounds + 1, first_rounds + 1, pair_rounds))]
                    n_doubles = [pool.value_load(doubles[0:1, n:n + 1], min_val=2, max_val=(seq // SLOTS + 1) // 2)
                                 for n in range(PAIR)]
                with pool.Fori(1, n_doubles[q]) as d:
                    gather_round(q, 0, d)
                    with pool.If(d * 2 + 1 < n_rounds[q]):
                        gather_round(q, 1, d)
                pool.wait_ge(rows_added[q], n_rounds[q] * SLOTS)
            for t in range(PAIR):
                gather_round(PAIR + t, t, 0)
            with pool.Fori(1, pair_rounds) as r:
                for t in range(PAIR):
                    gather_round(PAIR + t, t, r)
            with pool.If(n_rounds[2] > pair_rounds):
                with pool.Fori(pair_rounds, n_rounds[2]) as r:
                    for t in range(PAIR):
                        gather_round(PAIR + t, t, r)

        @block.tensor
        def _(pe):
            pe.wait_ge(counted, 2)
            pe.wait_ge(ident_made, 1)
            for q in range(tiles):
                mm = pe.matmul(count_ps[0:1, q * P:(q + 1) * P], count[:, q:q + 1], ident[:, :],
                               start=True, stop=True)
            mm.then_inc(counts_turned, 1)

            def turn_mean(q):
                pe.wait_ge(mean_steps[q], 2)
                for k in range(depth):
                    mm = pe.transpose(user_ps[q % PAIR][:, k, :], acc[:, q % PAIR, 0, k * P:(k + 1) * P], ident[:, :])
                mm.then_inc(mean_turned[q], 1)

            def user_parts_ready(q):
                pe.wait_ge(user_hi_ready[q], 1)
                pe.wait_ge(user_lo_ready[q], 1)

            def project(p, i, j, t, b, before):
                m = i + p * steps
                pe.wait_ge(w_hi_ready[j], m + 1 - p)
                pe.wait_ge(w_lo_ready[j], m + 1 - p)
                pe.wait_ge(out_copied[b], 2 * m + before + 1)
                if p == 0:
                    pe.matmul(out_ps[b][:, :], pick_row[:, j, :], bias_flat[:, bass.ds(i * chunk, chunk)],
                              start=True, stop=False)
                for k in range(depth):
                    hi, lo = user_hi[:, p * PAIR + t, k, :], user_lo[:, p * PAIR + t, k, :]
                    pe.matmul(out_ps[b][:, :], hi, w_hi[:, j, k, :], start=(p > 0 and k == 0), stop=False)
                    pe.matmul(out_ps[b][:, :], hi, w_lo[:, j, k, :], start=False, stop=False)
                    mm = pe.matmul(out_ps[b][:, :], lo, w_hi[:, j, k, :], start=False, stop=(k == depth - 1))
                mm.then_inc(out_summed[b], 1)

            turn_mean(0)
            pe.wait_ge(bias_rounded, 3)
            pe.wait_ge(pick_row_steps, 2)
            for t in range(PAIR):
                if t > 0:
                    turn_mean(t)
                user_parts_ready(t)
                for j in range(RING):
                    project(0, 0, j, t, *place_first(j, t))
            with pe.Fori(1, steps - 1) as i:
                for j in range(RING):
                    for t in range(PAIR):
                        project(0, i, j, t, *place(j, t))
            for j in range(RING):
                if j == RING - 1:
                    for t in range(PAIR):
                        turn_mean(PAIR + t)
                for t in range(PAIR):
                    project(0, steps - 1, j, t, *place(j, t))
            for t in range(PAIR):
                user_parts_ready(PAIR + t)
            with pe.Fori(0, steps) as i:
                for j in range(RING):
                    for t in range(PAIR):
                        project(1, i, j, t, *place(j, t))

        @block.scalar
        def _(act):
            for b in range(RING):
                act.sem_inc(out_copied[b], 1)
                act.sem_inc(out_stored[b], 16)

            def take_high(n, last, j):
                act.wait_ge(w_landed[j], 16 * n + 16)
                if last is not None:
                    b, before = (place_first if isinstance(last, int) and last == 0 else place)(j, PAIR - 1)
                    act.wait_ge(out_summed[b], 2 * last + 1 + before)
                act.activation(w_hi[:, j], w_raw[:, j], ACT.Copy).then_inc(w_hi_ready[j], 1)

            def user_high(q):
                act.wait_ge(mean_turned[q], 1)
                act.activation(user_hi[:, q], user_ps[q % PAIR][:, :, :], ACT.Copy).then_inc(user_hi_ready[q], 1)

            def copy_out(i, b, before):
                act.wait_ge(out_summed[b], 2 * i + before + 1)
                act.wait_ge(out_stored[b], 32 * i + 16 * before + 16)
                act.activation(out_sb[:, b, :], out_ps[b][:, :], ACT.Copy).then_inc(out_copied[b], 1)

            def store(p, i, j, t, b, before):
                act.wait_ge(out_copied[b], 2 * (i + p * steps) + before + 2)
                at = columns_back(i, j) if p > 0 else columns(i, j)
                act.dma_start(out_dram[(p * PAIR + t) * P:(p * PAIR + t + 1) * P, at],
                              out_sb[:, b, :]).then_inc(out_stored[b], 16)

            def put_out(i, j):
                for t in range(PAIR):
                    copy_out(i, *place(j, t))
                for t in range(PAIR):
                    store(0, i, j, t, *place(j, t))

            def load_bias(i, j):
                act.dma_start(bias_wide[:, j, :], bias_line[:, columns_back(i, j)].to_broadcast([P, chunk])
                              ).then_inc(bias_wide_landed[j], 16)

            for j in range(RING):
                take_high(0, None, j)
                if j == 1:
                    act.wait_ge(bias_cleared, 1)
                    act.wait_ge(bias_landed, 32)
                    for lo in (0, LOW):
                        act.activation(bias_parts[lo:lo + RING], bias_raw[lo:lo + RING], ACT.Copy
                                       ).then_inc(bias_rounded, 1)
            act.wait_ge(bias_rounded, 3)
            user_high(0)
            for t in range(PAIR):
                if t > 0:
                    user_high(t)
                for j in range(RING):
                    if t == PAIR - 1:
                        take_high(1, 0, j)
                    copy_out(0, *place_first(j, t))
                    if j > 0:
                        store(0, 0, j - 1, t, *place_first(j - 1, t))
                store(0, 0, RING - 1, t, *place_first(RING - 1, t))
            with act.Fori(1, steps - 1) as i:
                for j in range(RING):
                    take_high(i + 1, i, j)
                    put_out(i, j)
            for j in range(RING - 1):
                put_out(steps - 1, j)
            user_high(2)
            user_high(3)
            for j in range(RING):
                load_bias(0, j)
            put_out(steps - 1, RING - 1)
            with act.Fori(0, steps - 1) as i:
                for j in range(RING):
                    take_high(i + steps, i + steps, j)
                    for t in range(PAIR):
                        store(1, i, j, t, *place(j, t))
                    load_bias(i + 1, j)
            for j in range(RING):
                for t in range(PAIR):
                    store(1, steps - 1, j, t, *place(j, t))
            for b in range(RING):
                act.wait_ge(out_stored[b], 32 * passes * steps + 16)

        @block.vector
        def _(dve):
            taken = [[0] for _ in range(tiles)]
            ROUND_STEPS = 3

            def step(q, ins):
                taken[q][0] += 1
                ins.then_inc(sorted_steps[q], 1)

            def settled(q, base=0):
                dve.wait_ge(sorted_steps[q], base + taken[q][0])

            def refill(q, h, base=0):
                dve.tensor_scalar(pick[:, q, h, :], top[:, q, :], -1.0, float(items), ALU.mult, ALU.add
                                  ).then_inc(picks_ready[q][h], 1)
                step(q, dve.match_replace(keys[:, q, :], top[:, q, :], keys[:, q, :], 0.0))
                settled(q, base)
                step(q, dve.tensor_scalar(keep[:, q, h, :], pick[:, q, h, :], float(items), None, ALU.is_lt))
                step(q, dve.max(top[:, q, :], keys[:, q, :]))

            def first_refill(q, h):
                settled(q)
                step(q, dve.tensor_scalar(first[:, h, :], top[:, q, :], 1.0, None, ALU.max))
                settled(q)
                dve.tensor_scalar(pick[:, q, h, :], first[:, h, :], -1.0, float(items), ALU.mult, ALU.add
                                  ).then_inc(picks_ready[q][h], 1)
                step(q, dve.tensor_scalar(keep[:, q, h, :], top[:, q, :], 0.0, None, ALU.is_gt))
                step(q, dve.match_replace(keys[:, q, :], top[:, q, :], keys[:, q, :], 0.0))
                settled(q)
                step(q, dve.max(top[:, q, :], keys[:, q, :]))

            def add_rows(q, h, used, r, slots, between=()):
                for k in slots:
                    row, weight, total = rows[:, h, k, :], keep[:, q, h, k:k + 1], acc[:, q % PAIR, k % 2, :]
                    dve.wait_ge(row_landed[q][h][k], 16 * used + 16)
                    if isinstance(r, int) and r == 0 and k < 2:
                        dve.tensor_scalar(total, row, weight, None, ALU.mult).then_inc(rows_added[q], 1)
                    else:
                        dve.wait_ge(rows_added[q], SLOTS * r + k - 1)
                        dve.scalar_tensor_tensor(out=total, in0=row, scalar=weight, in1=total,
                                                 op0=ALU.mult, op1=ALU.add).then_inc(rows_added[q], 1)
                    for piece in between[k:k + 1]:
                        for j, d in piece:
                            low_piece(j, d)

            def end_round(q, h, r):
                dve.wait_ge(rows_added[q], SLOTS * r + SLOTS)
                settled(q, r * ROUND_STEPS)
                refill(q, h, r * ROUND_STEPS)
                taken[q][0] -= ROUND_STEPS

            def add_round(q, h, used, r, between=()):
                if isinstance(r, int) and r == 0:
                    settled(q)
                add_rows(q, h, used, r, range(SLOTS), between)
                end_round(q, h, r)

            def low_piece(j, d):
                if d == 0:
                    dve.wait_ge(w_hi_ready[j], 1)
                ins = dve.tensor_tensor(w_lo[:, j, d, :], w_raw[:, j, d, :], w_hi[:, j, d, :].bitcast(F32),
                                        ALU.subtract)
                if d == depth - 1:
                    ins.then_inc(w_lo_ready[j], 1)

            def take_low(n, j):
                dve.wait_ge(w_hi_ready[j], n + 1)
                dve.tensor_tensor(w_lo[:, j], w_raw[:, j], w_hi[:, j].bitcast(F32), ALU.subtract
                                  ).then_inc(w_lo_ready[j], 1)

            def mean(q):
                total = acc[:, q % PAIR, 0, :]
                dve.tensor_tensor(total, total, acc[:, q % PAIR, 1, :], ALU.add).then_inc(mean_steps[q], 1)
                dve.wait_ge(mean_steps[q], 1)
                dve.tensor_scalar(total, total, share[:, q:q + 1], None, ALU.mult).then_inc(mean_steps[q], 1)

            def user_low(q):
                dve.wait_ge(user_hi_ready[q], 1)
                dve.tensor_tensor(user_lo[:, q], user_ps[q % PAIR][:, :, :], user_hi[:, q].bitcast(F32), ALU.subtract
                                  ).then_inc(user_lo_ready[q], 1)

            dve.wait_ge(ids_landed, 16)
            for lot in (slice(0, 1), slice(1, tiles)):
                dve.tensor_scalar(keys[:, lot, :], ids[:, lot, :], -1.0, float(items), ALU.mult, ALU.add
                                  ).then_inc(keys_made, 1)
            dve.wait_ge(keys_made, 1)
            step(0, dve.max(top[:, 0, :], keys[:, 0, :]))
            dve.wait_ge(keys_made, 2)
            dve.tensor_scalar(valid, keys[:, :, :], 0.0, None, ALU.is_gt).then_inc(counted, 1)
            first_refill(0, 0)
            first_refill(0, 1)
            dve.tensor_reduce(count[:, :], valid, AX.X, ALU.add).then_inc(counted, 1)
            dve.wait_ge(ramps_made, 2)
            dve.tensor_scalar(ident[:, :], ramp_sq, 0.0, None, ALU.is_equal).then_inc(ident_made, 1)
            dve.tensor_scalar(pick_low, ramp, float(LOW), None, ALU.is_equal).then_inc(pick_row_steps, 1)
            for q in range(1, tiles):
                step(q, dve.max(top[:, q, :], keys[:, q, :]))
            dve.wait_ge(pick_row_steps, 1)
            dve.scalar_tensor_tensor(out=pick_row[:, :, :].rearrange("p j m -> p (j m)"), in0=ramp, scalar=0.0,
                                     in1=pick_low, op0=ALU.is_equal, op1=ALU.add).then_inc(pick_row_steps, 1)
            for q in range(1, tiles):
                settled(q)
                refill(q, q % 2 if q >= PAIR else 0)
            settled(1)
            refill(1, 1)

            dve.wait_ge(counted, 2)
            dve.tensor_scalar(denom[:, :], count[:, :], 1.0, None, ALU.max).then_inc(count_steps, 1)
            dve.wait_ge(count_steps, 1)
            dve.reciprocal(share[:, :], denom[:, :]).then_inc(count_steps, 1)
            dve.wait_ge(counts_turned, 1)
            dve.tensor_reduce(most[:, 0:PAIR], count_ps[0:1, 0:PAIR * P].rearrange("o (q u) -> o q u", q=PAIR),
                              AX.X, ALU.max).then_inc(count_steps, 1)
            dve.tensor_reduce(most[:, PAIR:PAIR + 1], count_ps[0:1, PAIR * P:], AX.X, ALU.max).then_inc(count_steps, 1)
            dve.wait_ge(count_steps, 4)
            for lot, least in ((slice(0, PAIR), first_rounds + 1), (slice(PAIR, PAIR + 1), pair_rounds)):
                dve.tensor_scalar(most_up[:, lot], most[:, lot], float(least * SLOTS), float(SLOTS - 1),
                                  ALU.max, ALU.add).then_inc(count_steps, 1)
            dve.tensor_scalar(doubles_up[:, :], most[:, 0:PAIR], float((first_rounds + 1) * SLOTS),
                              float(2 * SLOTS - 1), ALU.max, ALU.add).then_inc(count_steps, 1)
            dve.wait_ge(count_steps, 7)
            by = SLOTS.bit_length() - 1
            dve.tensor_scalar(rounds[:, :], most_up[:, :], by, None, ALU.logical_shift_right).then_inc(rounds_ready, 1)
            dve.tensor_scalar(doubles[:, :], doubles_up[:, :], by + 1, None, ALU.logical_shift_right
                              ).then_inc(rounds_ready, 1)

            pieces = [(j, d) for j in range(RING) for d in range(depth)]
            for q in range(PAIR):
                for h in range(first_rounds):
                    if q == 0 and h == 0:
                        dve.wait_ge(pick_row_steps, 2)
                        add_round(q, h, 0, h)
                        dve.wait_ge(bias_rounded, 2)
                        low = slice(LOW, LOW + RING)
                        dve.tensor_tensor(bias_parts[low], bias_raw[low], bias_parts[low].bitcast(F32), ALU.subtract
                                          ).then_inc(bias_rounded, 1)
                        dve.wait_ge(rounds_ready, 2)
                        n_rounds = [dve.value_load(rounds[0:1, n:n + 1], min_val=least, max_val=seq // SLOTS)
                                    for n, least in enumerate((first_rounds + 1, first_rounds + 1, pair_rounds))]
                        n_doubles = [dve.value_load(doubles[0:1, n:n + 1], min_val=2,
                                                    max_val=(seq // SLOTS + 1) // 2) for n in range(PAIR)]
                        continue
                    here = min(len(pieces), SLOTS - 1)
                    if q == 1 and h == 0:
                        add_rows(q, h, 0, h, range(0, 3))
                        user_low(0)
                        add_rows(q, h, 0, h, range(3, SLOTS), [[]] * 3 + [[x] for x in pieces[:5]])
                        del pieces[:5]
                        end_round(q, h, h)
                    else:
                        add_round(q, h, 0, h, [[x] for x in pieces[:here]])
                        del pieces[:here]
                with dve.Fori(1, n_doubles[q]) as d:
                    add_round(q, 0, d, d * 2)
                    with dve.If(d * 2 + 1 < n_rounds[q]):
                        add_round(q, 1, d, d * 2 + 1)
                mean(q)
            for piece in pieces:
                low_piece(*piece)
            user_low(1)

            def pair_part(i, j):
                if j == RING - 1:
                    return
                t, part = j // 2, j % 2
                add_rows(PAIR + t, t, i, i, range(part * SLOTS // 2, (part + 1) * SLOTS // 2))
                if part == 1:
                    end_round(PAIR + t, t, i)

            for j in range(RING):
                pair_part(0, j)
                take_low(1, j)
            with dve.Fori(1, steps - 1) as i:
                for j in range(RING):
                    pair_part(i, j)
                    take_low(i + 1, j)
            for j in range(RING):
                pair_part(steps - 1, j)
            with dve.If(n_rounds[2] > pair_rounds):
                with dve.Fori(pair_rounds, n_rounds[2]) as r:
                    for t in range(PAIR):
                        add_round(PAIR + t, t, r, r)
            mean(2)
            mean(3)
            user_low(2)
            user_low(3)

            def add_bias(i, j, b, before):
                m = i + steps
                dve.wait_ge(bias_wide_landed[j], 16 * i + 16)
                dve.wait_ge(out_stored[b], 32 * m + 16 * before + 16)
                dve.wait_ge(out_summed[b], 2 * m + before + 1)
                dve.tensor_tensor(out_sb[:, b, :], out_ps[b][:, :], bias_wide[:, j, :], ALU.add
                                  ).then_inc(out_copied[b], 1)

            with dve.Fori(0, steps - 1) as i:
                for j in range(RING):
                    for t in range(PAIR):
                        add_bias(i, j, *place(j, t))
                    take_low(i + steps, j)
            for j in range(RING):
                for t in range(PAIR):
                    add_bias(steps - 1, j, *place(j, t))


def kernel(r_sequence_ids, L0_rec_emb_table, L0_rec_proj_w, L0_rec_proj_b):
    import numpy as np
    import concourse.bacc as bacc
    from concourse.bass_utils import run_bass_kernel_spmd

    given = {"ids": r_sequence_ids, "table": L0_rec_emb_table, "weight": L0_rec_proj_w, "bias": L0_rec_proj_b}
    arrays = {f"{name}_dram": np.ascontiguousarray(a) for name, a in given.items()}
    nc = bacc.Bacc("TRN2", target_bir_lowering=False, num_devices=1)
    args = [nc.dram_tensor(name, a.shape, mybir.dt.from_np(a.dtype), kind="ExternalInput").ap()
            for name, a in arrays.items()]
    shape = (arrays["ids_dram"].shape[0], arrays["weight_dram"].shape[1])
    out = nc.dram_tensor("logits_dram", shape, F32, kind="ExternalOutput").ap()
    build_program(nc, *args, out)
    result = run_bass_kernel_spmd(nc, [arrays], core_ids=[0])
    return result.results[0]["logits_dram"]
```

```python
from contextlib import ExitStack

import concourse.bass as bass
from concourse import mybir

ALU = mybir.AluOpType
ACT = mybir.ActivationFunctionType
AX = mybir.AxisListType
F32 = mybir.dt.float32
F32R = mybir.dt.float32r
I32 = mybir.dt.int32
U32 = mybir.dt.uint32

P = 128
PAIR = 2
SLOTS = 8
HALF = SLOTS // 2
LEFT, RIGHT, ALL = range(HALF), range(HALF, SLOTS), range(SLOTS)
RING = 5
LOW = 32


def build_program(nc, ids_dram, table_dram, weight_dram, bias_dram, out_dram):
    users, seq = ids_dram.shape
    items, hidden = table_dram.shape
    tiles = users // P
    depth = hidden // P
    chunk = items // (RING * RING)
    steps = items // (chunk * RING)
    assert chunk * RING * steps == items and chunk <= 512 and chunk % 2 == 0 and tiles == 4 and steps == 5
    first_rounds = (3, 2)
    late_rounds = 5
    assert max(first_rounds[0] + 1, late_rounds) * SLOTS <= seq

    with ExitStack() as ctx:
        def sb(name, shape, dt):
            return ctx.enter_context(nc.sbuf_tensor(name, shape, dt))

        def ps(name, shape):
            return ctx.enter_context(nc.psum_tensor(name, shape, F32))

        def sem(name):
            return ctx.enter_context(nc.semaphore(name))

        ids = sb("ids", [P, tiles, seq], I32)
        keys = sb("keys", [P, tiles, seq], F32)
        top = sb("top", [P, tiles, SLOTS], F32)
        pick = sb("pick", [P, tiles, 2, SLOTS], I32)
        keep = sb("keep", [P, tiles, 2, SLOTS], F32)
        first = sb("first", [P, 2, SLOTS], F32)
        count = sb("count", [P, tiles], F32)
        denom = sb("denom", [P, tiles], F32)
        share = sb("share", [P, tiles], F32)
        most = sb("most", [1, tiles], F32)
        within = sb("within", [1, tiles], F32)
        most_up = sb("most_up", [1, tiles], I32)
        halves = sb("halves", [1, tiles], I32)
        loops_up = sb("loops_up", [1, tiles], I32)
        loops = sb("loops", [1, tiles], I32)
        valid = ids[:, :, :].bitcast(F32)

        rows = sb("rows", [P, 2, SLOTS, hidden], F32)
        acc = sb("acc", [P, PAIR, 2, hidden], F32)
        diagonals = acc[:, 1, :, :].rearrange("p a n -> p (a n)").rearrange("p (k m) -> p k m", m=P)
        user_hi = sb("user_hi", [P, tiles, depth, P], F32R)
        user_lo = sb("user_lo", [P, tiles, depth, P], F32R)

        w_raw = sb("w_raw", [P, RING, depth, chunk], F32)
        w_hi = sb("w_hi", [P, RING, depth, chunk], F32R)
        w_lo = sb("w_lo", [P, RING, depth, chunk], F32R)
        out_sb = sb("out_sb", [P, RING, chunk], F32)
        bias_parts = sb("bias_parts", [P, steps, chunk], F32R)
        bias_flat = bias_parts[:, :, :].rearrange("p i n -> p (i n)")
        bias_raw = out_sb[:, :, :]
        pick_row = sb("pick_row", [P, RING, P], F32R)
        ident = sb("ident", [P, P], F32)
        share_diagonal = sb("share_diagonal", [P, P], F32)
        room = w_raw[:, RING - 1, :, :].rearrange("p k n -> p (k n)")
        ramp = room[:, 0:RING * P].bitcast(I32)
        pick_low = room[:, RING * P:2 * RING * P]
        ramp_sq = room[:, 2 * RING * P:(2 * RING + 1) * P].bitcast(I32)
        bias_wide = rows[:, 0, :, :].rearrange("p k n -> p (k n)")[:, 0:RING * chunk].rearrange(
            "p (j n) -> p j n", n=chunk)
        bias_row = rows[0:1, 1, :, :].rearrange("p k n -> p (k n)")[:, 0:RING * chunk]

        out_ps = [ps(f"out_ps{b}", [P, chunk]) for b in range(RING)]
        user_ps = [ps(f"user_ps{t}", [P, depth, P]) for t in range(PAIR)]
        count_ps = ps("count_ps", [P, tiles * P])

        ids_landed = sem("ids_landed")
        bias_landed = sem("bias_landed")
        ramps_made = sem("ramps_made")
        keys_made = sem("keys_made")
        counted = sem("counted")
        count_steps = sem("count_steps")
        bias_cleared = sem("bias_cleared")
        pick_row_steps = sem("pick_row_steps")
        ident_made = sem("ident_made")
        bias_rounded = sem("bias_rounded")
        counts_turned = sem("counts_turned")
        rounds_ready = sem("rounds_ready")
        sorted_steps = [sem(f"sorted_steps{q}") for q in range(tiles)]
        picks_ready = [[sem(f"picks_ready{q}_{h}") for h in range(2)] for q in range(tiles)]
        row_landed = [[[sem(f"row_landed{q}_{h}_{k}") for k in range(SLOTS)] for h in range(2)]
                      for q in range(tiles)]
        acc_cleared = sem("acc_cleared")
        diagonals_ready = sem("diagonals_ready")
        share_diagonal_ready = sem("share_diagonal_ready")
        rows_summed = sem("rows_summed")
        tiles_landed = sem("tiles_landed")
        gathers_started = sem("gathers_started")
        rows_added = [sem(f"rows_added{q}") for q in range(tiles)]
        mean_steps = [sem(f"mean_steps{q}") for q in range(tiles)]
        mean_turned = [sem(f"mean_turned{q}") for q in range(tiles)]
        user_hi_ready = [sem(f"user_hi_ready{q}") for q in range(tiles)]
        user_lo_ready = [sem(f"user_lo_ready{q}") for q in range(tiles)]
        w_landed = [sem(f"w_landed{j}") for j in range(RING)]
        w_hi_ready = [sem(f"w_hi_ready{j}") for j in range(RING)]
        w_lo_ready = [sem(f"w_lo_ready{j}") for j in range(RING)]
        out_summed = [sem(f"out_summed{b}") for b in range(RING)]
        out_copied = [sem(f"out_copied{b}") for b in range(RING)]
        out_stored = [sem(f"out_stored{b}") for b in range(RING)]
        bias_row_landed = sem("bias_row_landed")
        spreads_started = sem("spreads_started")
        bias_wide_ready = [sem(f"bias_wide_ready{j}") for j in range(RING)]

        w_view = weight_dram.rearrange("(k p) n -> p k n", p=P)
        bias_view = bias_dram.rearrange("(i j n) -> j i n", j=RING, n=chunk)
        bias_line = bias_dram.rearrange("(o n) -> o n", o=1)
        block = ctx.enter_context(nc.Block())

        FIRST = ((0,), 0, 0, 0)
        SECOND = ((0, 1), 1, 1, 1)
        THIRD = ((0, 1), 3, 2, 2)
        FOURTH = ((0, 1), 5, 3, 3)
        FOURTH_2 = ((2,), 7, 3, 3)
        LAST = ((0, 1, 2), 8, 4, 4)
        BACK_LAST = ((3,), 11, 4, 4)
        BACK_FIRST = ((1, 2, 3), 12, 5, 0)
        BACK_FOURTH = ((3,), 15, 6, 3)
        BACK_PAIR = ((2, 3), 16, 7, 2)
        FORTH = (FIRST, SECOND, THIRD, FOURTH, FOURTH_2, LAST)
        all_uses = tiles * steps

        def place(leg, j, t):
            n = len(leg[0]) * j + t
            return n % RING, n // RING

        def place_first(leg, j, t):
            return j, t

        def uses(leg, i, before):
            return i * len(leg[0]) + (leg[1] + before)

        def columns(leg, i, j):
            return bass.ds(i * (-RING * chunk) + (leg[3] * RING + j) * chunk, chunk)

        def half(q, r):
            return (r + (q == 2)) % 2

        least_halves = tuple(2 * n + 1 for n in first_rounds) + (2 * late_rounds - 1,) * (tiles - PAIR)

        def load_counts(engine, q):
            return (engine.value_load(halves[0:1, q:q + 1], min_val=least_halves[q],
                                      max_val=seq // HALF if q < PAIR else 2 * late_rounds),
                    engine.value_load(loops[0:1, q:q + 1], min_val=(1, 2, 0, 0)[q],
                                      max_val=(seq // SLOTS + 1) // 2))

        @block.sync
        def _(sp):
            sp.dma_start(ids[:, :, :], ids_dram.rearrange("(t p) s -> p t s", p=P)).then_inc(ids_landed, 16)
            sp.dma_start(bias_raw[0:RING], bias_view).then_inc(bias_landed, 16)
            sp.dma_start(bias_raw[LOW:LOW + RING], bias_view).then_inc(bias_landed, 16)
            for j in range(RING):
                if 0 < j <= first_rounds[0]:
                    sp.wait_ge(row_landed[0][(j - 1) % 2][0], 16 * ((j - 1) // 2) + 16)
                elif j > 0:
                    sp.wait_ge(tiles_landed, 1)
                if j == RING - 1:
                    sp.wait_ge(ident_made, 1)
                    sp.wait_ge(pick_row_steps, 2)
                sp.dma_start(w_raw[:, j], w_view[:, :, columns(FIRST, 0, j)]).then_inc(w_landed[j], 16)

            def load(leg, i, j):
                n = i + leg[2]
                sp.wait_ge(w_hi_ready[j], n)
                sp.wait_ge(w_lo_ready[j], n)
                sp.dma_start(w_raw[:, j], w_view[:, :, columns(leg, i, j)]).then_inc(w_landed[j], 16)

            def load_bias(leg, i, m):
                if not (isinstance(m, int) and m == 0):
                    sp.wait_ge(bias_wide_ready[RING - 1], m)
                at = columns(leg, i, 0)
                sp.dma_start(bias_row, bias_line[:, bass.ds(at.start, RING * chunk)]).then_inc(bias_row_landed, 16)

            for j in range(RING):
                load(SECOND, 0, j)
            sp.wait_ge(tiles_landed, 2)
            for j in range(RING):
                load(THIRD, 0, j)
            for j in range(RING):
                sp.wait_ge(rows_added[2], HALF + j * HALF)
                load(FOURTH, 0, j)
            for q, leg in ((2, LAST), (3, BACK_FIRST)):
                sp.wait_ge(tiles_landed, q + 1)
                for j in range(RING):
                    load(leg, 0, j)
            sp.wait_ge(mean_steps[3], 1)
            load_bias(BACK_LAST, 0, 0)
            load_bias(BACK_FIRST, 0, 1)
            for j in range(RING):
                load(BACK_FOURTH, 0, j)
            load_bias(BACK_FOURTH, 0, 2)
            with sp.Fori(0, 2) as i:
                for j in range(RING):
                    load(BACK_PAIR, i, j)
                load_bias(BACK_PAIR, i, i + 3)

        @block.gpsimd
        def _(pool):
            pool.iota(ramp_sq, [[-1, P]], base=0, channel_multiplier=1).then_inc(ramps_made, 1)
            pool.iota(ramp.rearrange("p (j m) -> p j m", m=P), [[-1, RING], [0, P]], base=0,
                      channel_multiplier=1).then_inc(ramps_made, 1)
            pool.memset(bias_parts[:, :, :].bitcast(F32), 0.0).then_inc(bias_cleared, 1)

            def gather(q, h, slots):
                for k in slots:
                    pool.indirect_dma_start(
                        rows[:, h, k, :], None, table_dram,
                        bass.IndirectOffsetOnAxis(pick[:, q, h, k:k + 1].bitcast(U32), 0),
                        bounds_check=items - 1, oob_is_err=False).then_inc(row_landed[q][h][k], 16)

            def start_round(q, h, used):
                pool.wait_ge(picks_ready[q][h], used + 1)
                pool.sem_inc(gathers_started, 1)

            for r in range(first_rounds[0]):
                start_round(0, r % 2, r // 2)
                gather(0, r % 2, ALL)
            pool.wait_ge(rounds_ready, 2)
            counts = [load_counts(pool, q) for q in range(tiles)]
            n_halves, n_doubles = [c[0] for c in counts], [c[1] for c in counts]
            with pool.Fori(0, n_doubles[0]) as d:
                start_round(0, 1, d + 1)
                gather(0, 1, LEFT)
                with pool.If(n_halves[0] > d * 4 + 7):
                    gather(0, 1, RIGHT)
                    with pool.If(n_halves[0] > d * 4 + 8):
                        start_round(0, 0, d + 2)
                        gather(0, 0, LEFT)
                        with pool.If(n_halves[0] > d * 4 + 9):
                            gather(0, 0, RIGHT)

            pool.wait_ge(rows_summed, first_rounds[0] * SLOTS)
            with pool.If(n_halves[0] > 2 * (first_rounds[0] + 1)):
                pool.wait_ge(rows_added[0], n_halves[0] * HALF)
                pool.sem_inc(gathers_started, 1)
            start_round(1, 0, 0)
            gather(1, 0, ALL)
            pool.wait_ge(rows_added[0], n_halves[0] * HALF)
            pool.sem_inc(gathers_started, 1)
            start_round(1, 1, 0)
            gather(1, 1, ALL)
            with pool.Fori(1, n_doubles[1]) as d:
                start_round(1, 0, d)
                gather(1, 0, LEFT)
                with pool.If(n_halves[1] > d * 4 + 1):
                    gather(1, 0, RIGHT)
                    with pool.If(n_halves[1] > d * 4 + 2):
                        start_round(1, 1, d)
                        gather(1, 1, LEFT)
                        with pool.If(n_halves[1] > d * 4 + 3):
                            gather(1, 1, RIGHT)

            with pool.If(n_halves[1] > 7):
                pool.wait_ge(rows_added[1], 4 * SLOTS)
                pool.sem_inc(gathers_started, 1)
            with pool.If(n_halves[1] < 8):
                pool.wait_ge(rows_added[1], n_halves[1] * HALF)
                pool.sem_inc(gathers_started, 1)
            with pool.If(n_halves[1] > 10):
                pool.wait_ge(rows_added[1], n_halves[1] * HALF)
                pool.sem_inc(gathers_started, 1)
            for r in range(2):
                if r == 1:
                    pool.wait_ge(rows_added[1], n_halves[1] * HALF)
                    pool.sem_inc(gathers_started, 1)
                start_round(2, half(2, r), 0)
                gather(2, half(2, r), ALL)
            for r in range(2, 4):
                start_round(2, half(2, r), 1)
                gather(2, half(2, r), ALL)

            def spread_bias(leg, i, m, last_leg, last):
                pool.wait_ge(bias_row_landed, m * 16 + 16)
                for j in range(RING):
                    if last_leg is None:
                        pool.wait_ge(mean_steps[tiles - 1], 1)
                    else:
                        width = len(last_leg[0])
                        b, before = place(last_leg, j, width - 1)
                        pool.wait_ge(out_copied[b], uses(last_leg, last, before + 2 - width))
                    pool.sem_inc(spreads_started, 1)
                    pool.partition_broadcast(bias_wide[:, j, :], bias_row[:, j * chunk:(j + 1) * chunk]
                                             ).then_inc(bias_wide_ready[j], 1)

            def rest(q):
                last = late_rounds - 1
                start_round(q, half(q, last), last // 2)
                gather(q, half(q, last), LEFT)
                with pool.If(n_halves[q] > 2 * last + 1):
                    gather(q, half(q, last), RIGHT)
                with pool.If(n_doubles[q] > 0):
                    with pool.Fori(0, n_doubles[q]) as d:
                        for r in (late_rounds, late_rounds + 1):
                            start_round(q, half(q, r), d + r // 2)
                            gather(q, half(q, r), ALL)
                    pool.wait_ge(rows_added[q], n_doubles[q] * (2 * SLOTS) + late_rounds * SLOTS)
                    pool.sem_inc(gathers_started, 1)

            rest(2)
            pool.wait_ge(rows_added[2], (late_rounds - 1) * SLOTS)
            pool.wait_ge(w_landed[1], (LAST[2] + 1) * 16)
            start_round(3, half(3, 0), 0)
            gather(3, half(3, 0), ALL)
            pool.wait_ge(rows_added[2], n_halves[2] * HALF)
            pool.sem_inc(gathers_started, 1)
            start_round(3, half(3, 1), 0)
            gather(3, half(3, 1), ALL)
            for r in range(2, late_rounds - 1):
                start_round(3, half(3, r), r // 2)
                gather(3, half(3, r), ALL)
            rest(3)

            spread_bias(BACK_LAST, 0, 0, None, None)
            spread_bias(BACK_FIRST, 0, 1, BACK_LAST, 1)
            spread_bias(BACK_FOURTH, 0, 2, BACK_FIRST, 1)
            spread_bias(BACK_PAIR, 0, 3, BACK_FOURTH, 1)
            with pool.Fori(1, 2) as i:
                spread_bias(BACK_PAIR, i, i + 3, BACK_PAIR, i)

        @block.tensor
        def _(pe):
            pe.wait_ge(counted, 2)
            pe.wait_ge(ident_made, 1)
            for q in range(tiles):
                mm = pe.matmul(count_ps[0:1, q * P:(q + 1) * P], count[:, q:q + 1], ident[:, :],
                               start=True, stop=True)
            mm.then_inc(counts_turned, 1)

            for r in range(first_rounds[0]):
                for n in ALL:
                    pe.wait_ge(row_landed[0][r % 2][n], 16 * (r // 2) + 16)
                    pe.wait_ge(diagonals_ready, r * SLOTS + n + 1)
                    for k in range(depth):
                        mm = pe.matmul(user_ps[0][:, k, :], rows[:, r % 2, n, k * P:(k + 1) * P], diagonals[:, n, :],
                                       start=(r == 0 and n == 0 and k == 0), stop=False)
                    mm.then_inc(rows_summed, 1)
            pe.wait_ge(share_diagonal_ready, 1)
            pe.wait_ge(mean_steps[0], 1)
            for k in range(depth):
                mm = pe.matmul(user_ps[0][:, k, :], acc[:, 0, 0, k * P:(k + 1) * P], share_diagonal[:, :],
                               start=False, stop=(k == depth - 1))
            mm.then_inc(mean_turned[0], 1)

            def turn_mean(q):
                pe.wait_ge(mean_steps[q], 2)
                for k in range(depth):
                    mm = pe.transpose(user_ps[q % PAIR][:, k, :], acc[:, q % PAIR, 0, k * P:(k + 1) * P], ident[:, :])
                mm.then_inc(mean_turned[q], 1)

            def user_parts_ready(q):
                pe.wait_ge(user_hi_ready[q], 1)
                pe.wait_ge(user_lo_ready[q], 1)

            def project(leg, i, j, t, b, before):
                forth, q = leg in FORTH, leg[0][t]
                pe.wait_ge(w_hi_ready[j], i + (leg[2] + 1))
                pe.wait_ge(w_lo_ready[j], i + (leg[2] + 1))
                pe.wait_ge(out_copied[b], uses(leg, i, before) + 1)
                if forth:
                    at = bass.ds(i * chunk + leg[3] * chunk, chunk)
                    pe.matmul(out_ps[b][:, :], pick_row[:, j, :], bias_flat[:, at], start=True, stop=False)
                for k in range(depth):
                    hi, lo = user_hi[:, q, k, :], user_lo[:, q, k, :]
                    pe.matmul(out_ps[b][:, :], hi, w_hi[:, j, k, :], start=(not forth and k == 0), stop=False)
                    pe.matmul(out_ps[b][:, :], hi, w_lo[:, j, k, :], start=False, stop=False)
                    mm = pe.matmul(out_ps[b][:, :], lo, w_hi[:, j, k, :], start=False, stop=(k == depth - 1))
                mm.then_inc(out_summed[b], 1)

            def project_step(leg, i, turn=None):
                for j in range(RING):
                    for t in range(len(leg[0])):
                        if turn is not None and (j, t) == (RING - 1, len(leg[0]) - 1):
                            turn_mean(turn)
                        project(leg, i, j, t, *place(leg, j, t))

            pe.wait_ge(bias_rounded, 3)
            pe.wait_ge(pick_row_steps, 2)
            user_parts_ready(0)
            for leg, t in ((FIRST, 0), (SECOND, 0), (SECOND, 1)):
                if t == 1:
                    user_parts_ready(1)
                for j in range(RING):
                    if leg is SECOND and t == 0 and j == RING - 1:
                        turn_mean(1)
                    project(leg, 0, j, t, *place_first(leg, j, t))
            project_step(THIRD, 0)
            project_step(FOURTH, 0, turn=2)
            user_parts_ready(2)
            project_step(FOURTH_2, 0)
            project_step(LAST, 0, turn=3)
            user_parts_ready(3)
            for leg in (BACK_LAST, BACK_FIRST, BACK_FOURTH):
                project_step(leg, 0)
            with pe.Fori(0, 2) as i:
                project_step(BACK_PAIR, i)

        @block.scalar
        def _(act):
            for b in range(RING):
                act.sem_inc(out_copied[b], 1)
                act.sem_inc(out_stored[b], 16)

            def take_high(leg, i, j, where=place):
                if leg is None:
                    act.wait_ge(w_landed[j], 16)
                else:
                    act.wait_ge(w_landed[j], (i + (leg[2] + 1)) * 16 + 16)
                    b, before = where(leg, j, len(leg[0]) - 1)
                    act.wait_ge(out_summed[b], uses(leg, i, before) + 1)
                act.activation(w_hi[:, j], w_raw[:, j], ACT.Copy).then_inc(w_hi_ready[j], 1)

            def user_high(q):
                act.wait_ge(mean_turned[q], 1)
                act.activation(user_hi[:, q], user_ps[q % PAIR][:, :, :], ACT.Copy).then_inc(user_hi_ready[q], 1)

            def copy_out(leg, i, b, before):
                act.wait_ge(out_summed[b], uses(leg, i, before) + 1)
                act.wait_ge(out_stored[b], uses(leg, i, before) * 16 + 16)
                act.activation(out_sb[:, b, :], out_ps[b][:, :], ACT.Copy).then_inc(out_copied[b], 1)

            def store(leg, i, j, t, b, before):
                act.wait_ge(out_copied[b], uses(leg, i, before) + 2)
                q = leg[0][t]
                act.dma_start(out_dram[q * P:(q + 1) * P, columns(leg, i, j)], out_sb[:, b, :]
                              ).then_inc(out_stored[b], 16)

            def forth_step(leg, i, turned=None):
                width = len(leg[0])
                for j in range(RING):
                    for t in range(width):
                        if turned is not None and (j, t) == (RING - 1, width - 1):
                            user_high(turned)
                        if t == width - 1 and leg not in (FOURTH, LAST):
                            take_high(leg, i, j)
                        copy_out(leg, i, *place(leg, j, t))
                    for t in range(width):
                        store(leg, i, j, t, *place(leg, j, t))

            def back_step(leg, i, more=True):
                for j in range(RING):
                    if more:
                        take_high(leg, i, j)
                    for t in range(len(leg[0])):
                        store(leg, i, j, t, *place(leg, j, t))

            act.wait_ge(bias_cleared, 1)
            act.wait_ge(bias_landed, 32)
            for lo in (0, LOW):
                act.activation(bias_parts[lo:lo + RING], bias_raw[lo:lo + RING], ACT.Copy).then_inc(bias_rounded, 1)
            for j in range(RING):
                if j == 3:
                    user_high(0)
                take_high(None, 0, j)
            act.wait_ge(bias_rounded, 3)
            for leg, t in ((FIRST, 0), (SECOND, 0), (SECOND, 1)):
                for j in range(RING):
                    if leg is SECOND and t == 0 and j == RING - 1:
                        user_high(1)
                    if t == len(leg[0]) - 1:
                        take_high(leg, 0, j, place_first)
                    copy_out(leg, 0, *place_first(leg, j, t))
                    if j > 0:
                        store(leg, 0, j - 1, t, *place_first(leg, j - 1, t))
                store(leg, 0, RING - 1, t, *place_first(leg, RING - 1, t))
            forth_step(THIRD, 0)
            forth_step(FOURTH, 0, turned=2)
            forth_step(FOURTH_2, 0)
            forth_step(LAST, 0, turned=3)
            for leg in (BACK_LAST, BACK_FIRST, BACK_FOURTH, BACK_PAIR):
                back_step(leg, 0)
            back_step(BACK_PAIR, 1, more=False)
            for b in range(RING):
                act.wait_ge(out_stored[b], 16 * all_uses + 16)

        @block.vector
        def _(dve):
            taken = [[0] for _ in range(tiles)]
            ROUND_STEPS = 3

            def step(q, ins):
                taken[q][0] += 1
                ins.then_inc(sorted_steps[q], 1)

            def settled(q, base=0):
                dve.wait_ge(sorted_steps[q], base + taken[q][0])

            def refill(q, h, base=0):
                dve.tensor_scalar(pick[:, q, h, :], top[:, q, :], -1.0, float(items), ALU.mult, ALU.add
                                  ).then_inc(picks_ready[q][h], 1)
                step(q, dve.match_replace(keys[:, q, :], top[:, q, :], keys[:, q, :], 0.0))
                settled(q, base)
                step(q, dve.tensor_scalar(keep[:, q, h, :], pick[:, q, h, :], float(items), None, ALU.is_lt))
                step(q, dve.max(top[:, q, :], keys[:, q, :]))

            def first_refill(q, h):
                settled(q)
                step(q, dve.tensor_scalar(first[:, h, :], top[:, q, :], 1.0, None, ALU.max))
                settled(q)
                dve.tensor_scalar(pick[:, q, h, :], first[:, h, :], -1.0, float(items), ALU.mult, ALU.add
                                  ).then_inc(picks_ready[q][h], 1)
                step(q, dve.tensor_scalar(keep[:, q, h, :], top[:, q, :], 0.0, None, ALU.is_gt))
                step(q, dve.match_replace(keys[:, q, :], top[:, q, :], keys[:, q, :], 0.0))
                settled(q)
                step(q, dve.max(top[:, q, :], keys[:, q, :]))

            def add_rows(q, h, used, r, slots, between={}):
                for k in slots:
                    row, weight, total = rows[:, h, k, :], keep[:, q, h, k:k + 1], acc[:, q % PAIR, k % 2, :]
                    dve.wait_ge(row_landed[q][h][k], 16 * used + 16)
                    if isinstance(r, int) and r == 0 and k < 2:
                        dve.tensor_scalar(total, row, weight, None, ALU.mult).then_inc(rows_added[q], 1)
                    else:
                        dve.wait_ge(rows_added[q], SLOTS * r + k - 1)
                        dve.scalar_tensor_tensor(out=total, in0=row, scalar=weight, in1=total,
                                                 op0=ALU.mult, op1=ALU.add).then_inc(rows_added[q], 1)
                    for n, j in between.get(k, ()):
                        take_low(n, j)

            def end_round(q, h, r, used=None):
                dve.wait_ge(used or rows_added[q], SLOTS * r + SLOTS)
                settled(q, r * ROUND_STEPS)
                refill(q, h, r * ROUND_STEPS)
                taken[q][0] -= ROUND_STEPS

            def add_round(q, h, used, r, between={}):
                if isinstance(r, int) and r == 0:
                    settled(q)
                add_rows(q, h, used, r, ALL, between)
                end_round(q, h, r)

            def take_low(n, j):
                dve.wait_ge(w_hi_ready[j], n + 1)
                dve.tensor_tensor(w_lo[:, j], w_raw[:, j], w_hi[:, j].bitcast(F32), ALU.subtract
                                  ).then_inc(w_lo_ready[j], 1)

            def make_diagonals(r):
                settled(0, max(r - 1, 0) * ROUND_STEPS)
                for k in ALL:
                    if r > 0:
                        dve.wait_ge(rows_summed, SLOTS * (r - 1) + k + 1)
                    dve.tensor_scalar(diagonals[:, k, :], ident[:, :], keep[:, 0, r % 2, k:k + 1], share[:, 0:1],
                                      ALU.mult, ALU.mult).then_inc(diagonals_ready, 1)

            def mean(q):
                total = acc[:, q % PAIR, 0, :]
                dve.tensor_tensor(total, total, acc[:, q % PAIR, 1, :], ALU.add).then_inc(mean_steps[q], 1)
                dve.wait_ge(mean_steps[q], 1)
                dve.tensor_scalar(total, total, share[:, q:q + 1], None, ALU.mult).then_inc(mean_steps[q], 1)

            def user_low(q):
                dve.wait_ge(user_hi_ready[q], 1)
                dve.tensor_tensor(user_lo[:, q], user_ps[q % PAIR][:, :, :], user_hi[:, q].bitcast(F32), ALU.subtract
                                  ).then_inc(user_lo_ready[q], 1)

            dve.wait_ge(ids_landed, 16)
            for lot in (slice(0, 1), slice(1, tiles)):
                dve.tensor_scalar(keys[:, lot, :], ids[:, lot, :], -1.0, float(items), ALU.mult, ALU.add
                                  ).then_inc(keys_made, 1)
            dve.wait_ge(keys_made, 1)
            step(0, dve.max(top[:, 0, :], keys[:, 0, :]))
            dve.wait_ge(keys_made, 2)
            dve.tensor_scalar(valid, keys[:, :, :], 0.0, None, ALU.is_gt).then_inc(counted, 1)
            first_refill(0, 0)
            first_refill(0, 1)
            dve.tensor_reduce(count[:, :], valid, AX.X, ALU.add).then_inc(counted, 1)
            dve.wait_ge(ramps_made, 2)
            dve.tensor_scalar(ident[:, :], ramp_sq, 0.0, None, ALU.is_equal).then_inc(ident_made, 1)
            dve.wait_ge(counted, 2)
            dve.tensor_scalar(denom[:, :], count[:, :], 1.0, None, ALU.max).then_inc(count_steps, 1)
            dve.tensor_scalar(pick_low, ramp, float(LOW), None, ALU.is_equal).then_inc(pick_row_steps, 1)
            dve.wait_ge(count_steps, 1)
            dve.reciprocal(share[:, :], denom[:, :]).then_inc(count_steps, 1)
            dve.memset(acc[:, 0, :, :], 0.0).then_inc(acc_cleared, 1)
            dve.wait_ge(count_steps, 2)
            dve.wait_ge(ident_made, 1)
            make_diagonals(0)
            dve.wait_ge(pick_row_steps, 1)
            dve.scalar_tensor_tensor(out=pick_row[:, :, :].rearrange("p j m -> p (j m)"), in0=ramp, scalar=0.0,
                                     in1=pick_low, op0=ALU.is_equal, op1=ALU.add).then_inc(pick_row_steps, 1)
            dve.tensor_scalar(share_diagonal[:, :], ident[:, :], share[:, 0:1], None, ALU.mult
                              ).then_inc(share_diagonal_ready, 1)

            dve.wait_ge(counts_turned, 1)
            dve.tensor_reduce(most[:, :], count_ps[0:1, :].rearrange("o (q u) -> o q u", q=tiles), AX.X, ALU.max
                              ).then_inc(count_steps, 1)
            dve.wait_ge(count_steps, 3)
            others = slice(PAIR, tiles)
            least = [(n - 1) * HALF + 1.0 for n in least_halves]
            whole = float(late_rounds * SLOTS)
            for q in range(PAIR):
                dve.tensor_scalar(within[:, q:q + 1], most[:, q:q + 1], least[q], None, ALU.max
                                  ).then_inc(count_steps, 1)
            dve.tensor_scalar(within[:, others], most[:, others], least[PAIR], whole, ALU.max, ALU.min
                              ).then_inc(count_steps, 1)
            dve.tensor_scalar(loops_up[:, others], most[:, others], whole, 2 * SLOTS - 1 - whole, ALU.max, ALU.add
                              ).then_inc(count_steps, 1)
            dve.wait_ge(count_steps, 7)
            dve.tensor_scalar(most_up[:, :], within[:, :], HALF - 1.0, None, ALU.add).then_inc(count_steps, 1)
            for q, before in ((0, first_rounds[0] * SLOTS), (1, 0)):
                dve.tensor_scalar(loops_up[:, q:q + 1], within[:, q:q + 1], 2 * SLOTS - 1.0 - before, None, ALU.add
                                  ).then_inc(count_steps, 1)
            dve.wait_ge(count_steps, 10)
            for to, up, part in ((halves, most_up, HALF), (loops, loops_up, 2 * SLOTS)):
                dve.tensor_scalar(to[:, :], up[:, :], part.bit_length() - 1, None, ALU.logical_shift_right
                                  ).then_inc(rounds_ready, 1)

            make_diagonals(1)
            end_round(0, 0, 0, rows_summed)
            for q in (1, 2):
                step(q, dve.max(top[:, q, :], keys[:, q, :]))
            for r in range(2):
                for q in (1, 2):
                    settled(q)
                    refill(q, half(q, r))
            dve.wait_ge(bias_rounded, 2)
            low = slice(LOW, LOW + RING)
            dve.tensor_tensor(bias_parts[low], bias_raw[low], bias_parts[low].bitcast(F32), ALU.subtract
                              ).then_inc(bias_rounded, 1)
            take_low(0, 0)
            make_diagonals(2)
            end_round(0, 1, 1, rows_summed)
            dve.wait_ge(rounds_ready, 2)
            halves_0, doubles_0 = load_counts(dve, 0)
            take_low(0, 1)
            end_round(0, 0, 2, rows_summed)
            dve.sem_inc(rows_added[0], first_rounds[0] * SLOTS)
            dve.wait_ge(acc_cleared, 1)
            with dve.Fori(0, doubles_0) as d:
                add_rows(0, 1, d + 1, d * 2 + 3, LEFT)
                with dve.If(halves_0 > d * 4 + 7):
                    add_rows(0, 1, d + 1, d * 2 + 3, RIGHT)
                    with dve.If(halves_0 > d * 4 + 8):
                        end_round(0, 1, d * 2 + 3)
                        add_rows(0, 0, d + 2, d * 2 + 4, LEFT)
                        with dve.If(halves_0 > d * 4 + 9):
                            add_rows(0, 0, d + 2, d * 2 + 4, RIGHT)
                            end_round(0, 0, d * 2 + 4)
            dve.sem_inc(tiles_landed, 1)
            dve.wait_ge(rows_added[0], halves_0 * HALF)
            dve.tensor_tensor(acc[:, 0, 0, :], acc[:, 0, 0, :], acc[:, 0, 1, :], ALU.add).then_inc(mean_steps[0], 1)
            take_low(0, 2)
            user_low(0)

            settled(1)
            add_rows(1, 0, 0, 0, ALL, {1: [(0, 3)], 4: [(0, 4)], 7: [(1, 0)]})
            end_round(1, 0, 0)
            add_round(1, 1, 0, 1, {1: [(1, 1)], 4: [(1, 2)], 7: [(1, 3)]})
            halves_1, doubles_1 = load_counts(dve, 1)
            with dve.Fori(1, doubles_1) as d:
                add_rows(1, 0, d, d * 2, LEFT)
                with dve.If(halves_1 > d * 4 + 1):
                    add_rows(1, 0, d, d * 2, RIGHT)
                    end_round(1, 0, d * 2)
                    with dve.If(halves_1 > d * 4 + 2):
                        add_rows(1, 1, d, d * 2 + 1, LEFT)
                        with dve.If(halves_1 > d * 4 + 3):
                            add_rows(1, 1, d, d * 2 + 1, RIGHT)
                            end_round(1, 1, d * 2 + 1)
            dve.sem_inc(tiles_landed, 1)
            dve.wait_ge(rows_added[1], halves_1 * HALF)
            mean(1)
            take_low(1, 4)
            user_low(1)

            def half_round(q, r, part):
                add_rows(q, half(q, r), r // 2, r, (LEFT, RIGHT)[part])
                if part == 1:
                    end_round(q, half(q, r), r)

            def rest(q):
                last = late_rounds - 1
                halves_q, doubles_q = load_counts(dve, q)
                add_rows(q, half(q, last), last // 2, last, LEFT)
                with dve.If(halves_q > 2 * last + 1):
                    add_rows(q, half(q, last), last // 2, last, RIGHT)
                    end_round(q, half(q, last), last)
                with dve.If(doubles_q > 0):
                    with dve.Fori(0, doubles_q) as d:
                        for r in (late_rounds, late_rounds + 1):
                            add_round(q, half(q, r), d + r // 2, d * 2 + r)
                dve.sem_inc(tiles_landed, 1)
                dve.wait_ge(rows_added[q], last * SLOTS + HALF)

            for j in range(RING):
                if j < RING - 1:
                    half_round(2, j // 2, j % 2)
                take_low(2, j)
            step(3, dve.max(top[:, 3, :], keys[:, 3, :]))
            for r in range(2):
                settled(3)
                refill(3, half(3, r))
            for j in range(RING):
                if j < RING - 1:
                    half_round(2, 2 + j // 2, j % 2)
                take_low(3, j)
            rest(2)
            mean(2)
            user_low(2)
            for j in range(RING):
                take_low(4, j)
                half_round(3, j // 2, j % 2)
            half_round(3, 2, 1)
            half_round(3, 3, 0)
            half_round(3, 3, 1)
            rest(3)
            mean(3)
            user_low(3)

            def add_bias(leg, i, m, j, b, before):
                dve.wait_ge(bias_wide_ready[j], m + 1)
                dve.wait_ge(out_stored[b], uses(leg, i, before) * 16 + 16)
                dve.wait_ge(out_summed[b], uses(leg, i, before) + 1)
                dve.tensor_tensor(out_sb[:, b, :], out_ps[b][:, :], bias_wide[:, j, :], ALU.add
                                  ).then_inc(out_copied[b], 1)

            def back_step(leg, i, m, more=True):
                for j in range(RING):
                    for t in range(len(leg[0])):
                        add_bias(leg, i, m, j, *place(leg, j, t))
                    if more:
                        take_low(i + (leg[2] + 1), j)

            back_step(BACK_LAST, 0, 0)
            back_step(BACK_FIRST, 0, 1)
            back_step(BACK_FOURTH, 0, 2)
            back_step(BACK_PAIR, 0, 3)
            back_step(BACK_PAIR, 1, 4, more=False)


def kernel(r_sequence_ids, L0_rec_emb_table, L0_rec_proj_w, L0_rec_proj_b):
    import numpy as np
    import concourse.bacc as bacc
    from concourse.bass_utils import run_bass_kernel_spmd

    given = {"ids": r_sequence_ids, "table": L0_rec_emb_table, "weight": L0_rec_proj_w, "bias": L0_rec_proj_b}
    arrays = {f"{name}_dram": np.ascontiguousarray(a) for name, a in given.items()}
    nc = bacc.Bacc("TRN2", target_bir_lowering=False, num_devices=1)
    args = [nc.dram_tensor(name, a.shape, mybir.dt.from_np(a.dtype), kind="ExternalInput").ap()
            for name, a in arrays.items()]
    shape = (arrays["ids_dram"].shape[0], arrays["weight_dram"].shape[1])
    out = nc.dram_tensor("logits_dram", shape, F32, kind="ExternalOutput").ap()
    build_program(nc, *args, out)
    result = run_bass_kernel_spmd(nc, [arrays], core_ids=[0])
    return result.results[0]["logits_dram"]
```
